# Optimizing a Trainium2 kernel written in Bass

```python
import numpy as np
import jax
import jax.numpy as jnp

def _softmax(x, axis=-1):
    return jax.nn.softmax(x, axis=axis)

def _gelu(x):
    return jax.nn.gelu(x, approximate=True)

def _silu(x):
    return jax.nn.silu(x)

def _sigmoid(x):
    return jax.nn.sigmoid(x)

def _layernorm(x, axis=-1, eps=1e-05):
    m = jnp.mean(x, axis=axis, keepdims=True)
    v = jnp.var(x, axis=axis, keepdims=True)
    return (x - m) / jnp.sqrt(v + eps)

def _scatter_add(tgt, idx, src, axis=0):
    return tgt.at[idx].add(src)

def _segment_sum(src, seg, n):
    return jax.ops.segment_sum(src, seg, n)
kernel_name = 'mk_perceiver_d1_seqx_r2_18a80c'

def setup_inputs(seed: int=0):
    np.random.seed(seed)
    _w = jnp.asarray

    def _rec_inputs():
        import jax
        import jax.numpy as jnp
        _rk = jax.random.key(seed)
        x = -0.0003929 + 0.9999 * jax.random.normal(jax.random.fold_in(_rk, 1), (4, 128, 512), jnp.float32)
        _lenS = 128 - jax.random.randint(jax.random.fold_in(_rk, 7), (4,), 0, max(1, 128 // 4) + 1, jnp.int32)
        _lenS2 = 2048 - jax.random.randint(jax.random.fold_in(_rk, 8), (4,), 0, max(1, 2048 // 4) + 1, jnp.int32)
        _ctx_768P = jax.random.normal(jax.random.fold_in(_rk, 11), (4, 16, 384), jnp.float32)
        _ctx_768c = jax.random.dirichlet(jax.random.fold_in(_rk, 511), 0.3 * jnp.ones((16,), jnp.float32), (4, 2048))
        _ctx_768t = jnp.einsum('bsk,bkd->bsd', _ctx_768c, _ctx_768P)
        _ctx_768t = _ctx_768t * jax.lax.rsqrt(jnp.mean(jnp.square(_ctx_768t)) + 1e-12) * 0.953939
        ctx_768 = -7.36909e-05 + 0.999899 * (_ctx_768t + 0.3 * jax.random.normal(jax.random.fold_in(_rk, 611), (4, 2048, 384), jnp.float32))
        return (x, ctx_768)
    x, ctx_768 = _rec_inputs()

    def _L0_xattn_setup():
        import jax, jax.numpy as jnp
        import numpy as np
        IMG_DIM, TXT_DIM, HID = (512, 384, 512)
        B, LQ, LK = (8, 1024, 1024)
        key = jax.random.key(seed)
        ks = jax.random.split(key, 8)
        s_img = 1.0 / np.sqrt(IMG_DIM)
        s_txt = 1.0 / np.sqrt(TXT_DIM)
        return {'image_features': jax.random.normal(ks[0], (B, LQ, IMG_DIM), jnp.float32), 'text_features': jax.random.normal(ks[1], (B, LK, TXT_DIM), jnp.float32), 'Wq': jax.random.uniform(ks[2], (IMG_DIM, HID), jnp.float32, -s_img, s_img), 'bq': jax.random.uniform(ks[3], (HID,), jnp.float32, -s_img, s_img), 'Wk': jax.random.uniform(ks[4], (TXT_DIM, HID), jnp.float32, -s_txt, s_txt), 'bk': jax.random.uniform(ks[5], (HID,), jnp.float32, -s_txt, s_txt), 'Wv': jax.random.uniform(ks[6], (TXT_DIM, HID), jnp.float32, -s_txt, s_txt), 'bv': jax.random.uniform(ks[7], (HID,), jnp.float32, -s_txt, s_txt)}
    _L0_xattn_all = _L0_xattn_setup()
    _L0_xattn_in = {k: v for k, v in _L0_xattn_all.items() if k in ('Wq', 'bq', 'Wk', 'bk', 'Wv', 'bv')}
    del _L0_xattn_all

    def _L0_attn_setup():
        import jax, jax.numpy as jnp
        import numpy as np
        import math
        D_MODEL = 512
        N_HEADS = 16
        Q_PROJ = D_MODEL // 4
        KV_PROJ = D_MODEL // 4
        DH = D_MODEL // N_HEADS
        LN_EPS = 1e-05

        def _layernorm(x, gamma, beta):
            mu = jnp.mean(x, axis=-1, keepdims=True)
            var = jnp.mean(jnp.square(x - mu), axis=-1, keepdims=True)
            return (x - mu) * jax.lax.rsqrt(var + LN_EPS) * gamma + beta
        key = jax.random.key(seed)
        ks = jax.random.split(key, 7)
        B, S = (2, 1024)
        x = jax.random.normal(ks[0], (B, S, D_MODEL), dtype=jnp.float32)
        W_dq = 0.01 * jax.random.normal(ks[1], (D_MODEL, Q_PROJ), dtype=jnp.float32)
        W_uq = 0.01 * jax.random.normal(ks[2], (Q_PROJ, D_MODEL), dtype=jnp.float32)
        W_dkv = 0.01 * jax.random.normal(ks[3], (D_MODEL, KV_PROJ), dtype=jnp.float32)
        W_ukv = 0.01 * jax.random.normal(ks[4], (KV_PROJ, 2 * D_MODEL), dtype=jnp.float32)
        W_o = 0.01 * jax.random.normal(ks[5], (D_MODEL, D_MODEL), dtype=jnp.float32)
        return {'x': x, 'W_dq': W_dq, 'W_uq': W_uq, 'q_ln_g': jnp.ones((Q_PROJ,), jnp.float32), 'q_ln_b': jnp.zeros((Q_PROJ,), jnp.float32), 'W_dkv': W_dkv, 'W_ukv': W_ukv, 'kv_ln_g': jnp.ones((KV_PROJ,), jnp.float32), 'kv_ln_b': jnp.zeros((KV_PROJ,), jnp.float32), 'W_o': W_o}
    _L0_attn_all = _L0_attn_setup()
    _L0_attn_in = {k: v for k, v in _L0_attn_all.items() if k in ('W_dq', 'W_uq', 'q_ln_g', 'q_ln_b', 'W_dkv', 'W_ukv', 'kv_ln_g', 'kv_ln_b', 'W_o')}
    del _L0_attn_all

    def _L0_ffn_setup():
        import jax, jax.numpy as jnp
        import numpy as np
        DIM = 512
        N_EXPERTS = 16
        TOP_K = 4
        N_GROUP = 4
        TOPK_GROUP = 2
        MOE_INTER = 256
        SHARED_INTER = 1024
        ROUTED_SCALE = 2.5

        def relu2(x):
            return jnp.square(jax.nn.relu(x))

        def _router(x2, gate_w, bias_e):
            T = x2.shape[0]
            logits = x2 @ gate_w.T
            scores = jax.nn.sigmoid(logits)
            sc = jax.lax.stop_gradient(scores + bias_e[None, :])
            grp = sc.reshape(T, N_GROUP, N_EXPERTS // N_GROUP)
            top2, _ = jax.lax.top_k(grp, 2)
            group_scores = top2.sum(-1)
            _, gidx = jax.lax.top_k(group_scores, TOPK_GROUP)
            rows = jnp.arange(T)[:, None]
            gmask = jnp.zeros((T, N_GROUP), dtype=sc.dtype).at[rows, gidx].set(1.0)
            smask = jnp.repeat(gmask, N_EXPERTS // N_GROUP, axis=1)
            masked = jnp.where(smask > 0, sc, 0.0)
            _, topk_idx = jax.lax.top_k(masked, TOP_K)
            topk_w = jnp.take_along_axis(scores, topk_idx, axis=1)
            topk_w = topk_w / (topk_w.sum(-1, keepdims=True) + 1e-20)
            topk_w = topk_w * ROUTED_SCALE
            return (topk_idx, topk_w)
        key = jax.random.key(seed)
        ks = jax.random.split(key, 6)
        hidden_states = jax.random.normal(ks[0], (2, 1024, DIM), dtype=jnp.float32)
        gate_w = jax.random.normal(ks[1], (N_EXPERTS, DIM), dtype=jnp.float32) * 0.02
        bias_e = jnp.zeros((N_EXPERTS,), dtype=jnp.float32)
        up_w = jax.random.normal(ks[2], (N_EXPERTS, MOE_INTER, DIM), dtype=jnp.float32) * 0.02
        down_w = jax.random.normal(ks[3], (N_EXPERTS, DIM, MOE_INTER), dtype=jnp.float32) * 0.02
        shared_up = jax.random.normal(ks[4], (SHARED_INTER, DIM), dtype=jnp.float32) * 0.02
        shared_down = jax.random.normal(ks[5], (DIM, SHARED_INTER), dtype=jnp.float32) * 0.02
        return {'hidden_states': hidden_states, 'gate_w': gate_w, 'bias_e': bias_e, 'up_w': up_w, 'down_w': down_w, 'shared_up': shared_up, 'shared_down': shared_down}
    _L0_ffn_all = _L0_ffn_setup()
    _L0_ffn_in = {k: v for k, v in _L0_ffn_all.items() if k in ('gate_w', 'bias_e', 'up_w', 'down_w', 'shared_up', 'shared_down')}
    del _L0_ffn_all
    return {'x': x, 'ctx_768': ctx_768, 'L0_xattn_Wq': _L0_xattn_in['Wq'], 'L0_xattn_bq': _L0_xattn_in['bq'], 'L0_xattn_Wk': _L0_xattn_in['Wk'], 'L0_xattn_bk': _L0_xattn_in['bk'], 'L0_xattn_Wv': _L0_xattn_in['Wv'], 'L0_xattn_bv': _L0_xattn_in['bv'], 'L0_attn_W_dq': _L0_attn_in['W_dq'], 'L0_attn_W_uq': _L0_attn_in['W_uq'], 'L0_attn_q_ln_g': _L0_attn_in['q_ln_g'], 'L0_attn_q_ln_b': _L0_attn_in['q_ln_b'], 'L0_attn_W_dkv': _L0_attn_in['W_dkv'], 'L0_attn_W_ukv': _L0_attn_in['W_ukv'], 'L0_attn_kv_ln_g': _L0_attn_in['kv_ln_g'], 'L0_attn_kv_ln_b': _L0_attn_in['kv_ln_b'], 'L0_attn_W_o': _L0_attn_in['W_o'], 'L0_ffn_gate_w': _L0_ffn_in['gate_w'], 'L0_ffn_bias_e': _L0_ffn_in['bias_e'], 'L0_ffn_up_w': _L0_ffn_in['up_w'], 'L0_ffn_down_w': _L0_ffn_in['down_w'], 'L0_ffn_shared_up': _L0_ffn_in['shared_up'], 'L0_ffn_shared_down': _L0_ffn_in['shared_down']}

def reference(x, ctx_768, L0_xattn_Wq, L0_xattn_bq, L0_xattn_Wk, L0_xattn_bk, L0_xattn_Wv, L0_xattn_bv, L0_attn_W_dq, L0_attn_W_uq, L0_attn_q_ln_g, L0_attn_q_ln_b, L0_attn_W_dkv, L0_attn_W_ukv, L0_attn_kv_ln_g, L0_attn_kv_ln_b, L0_attn_W_o, L0_ffn_gate_w, L0_ffn_bias_e, L0_ffn_up_w, L0_ffn_down_w, L0_ffn_shared_up, L0_ffn_shared_down):
    import jax
    import jax.numpy as jnp

    def _L0_xattn_ref(image_features, text_features, Wq, bq, Wk, bk, Wv, bv):
        import jax, jax.numpy as jnp
        import numpy as np
        IMG_DIM, TXT_DIM, HID = (512, 384, 512)
        B, LQ, LK = (8, 1024, 1024)
        query = jnp.einsum('bqi,ih->bqh', image_features, Wq) + bq
        key = jnp.einsum('bkt,th->bkh', text_features, Wk) + bk
        value = jnp.einsum('bkt,th->bkh', text_features, Wv) + bv
        scale = 1.0 / jnp.sqrt(jnp.asarray(HID, query.dtype))
        scores = jnp.einsum('bqh,bkh->bqk', query, key) * scale
        weights = jax.nn.softmax(scores, axis=-1)
        attended = jnp.einsum('bqk,bkh->bqh', weights, value)
        return attended

    def _L0_attn_ref(x, W_dq, W_uq, q_ln_g, q_ln_b, W_dkv, W_ukv, kv_ln_g, kv_ln_b, W_o):
        import jax, jax.numpy as jnp
        import numpy as np
        import math
        D_MODEL = 512
        N_HEADS = 16
        Q_PROJ = D_MODEL // 4
        KV_PROJ = D_MODEL // 4
        DH = D_MODEL // N_HEADS
        LN_EPS = 1e-05

        def _layernorm(x, gamma, beta):
            mu = jnp.mean(x, axis=-1, keepdims=True)
            var = jnp.mean(jnp.square(x - mu), axis=-1, keepdims=True)
            return (x - mu) * jax.lax.rsqrt(var + LN_EPS) * gamma + beta
        B, S, D = x.shape
        cq = _layernorm(x @ W_dq, q_ln_g, q_ln_b)
        Q = cq @ W_uq
        ckv = _layernorm(x @ W_dkv, kv_ln_g, kv_ln_b)
        KV = ckv @ W_ukv
        K, V = (KV[..., :D], KV[..., D:])
        q = Q.reshape(B, S, N_HEADS, DH)
        k = K.reshape(B, S, N_HEADS, DH)
        v = V.reshape(B, S, N_HEADS, DH)
        scores = jnp.einsum('bqhd,bkhd->bhqk', q, k) / math.sqrt(float(DH))
        mask = jnp.tril(jnp.ones((S, S), dtype=scores.dtype))
        scores = scores * mask
        scores = jnp.where(scores == 0, -jnp.inf, scores)
        attn = jax.nn.softmax(scores, axis=-1)
        out = jnp.einsum('bhqk,bkhd->bqhd', attn, v).reshape(B, S, D)
        return out @ W_o.T

    def _L0_ffn_ref(hidden_states, gate_w, bias_e, up_w, down_w, shared_up, shared_down):
        import jax, jax.numpy as jnp
        import numpy as np
        DIM = 512
        N_EXPERTS = 16
        TOP_K = 4
        N_GROUP = 4
        TOPK_GROUP = 2
        MOE_INTER = 256
        SHARED_INTER = 1024
        ROUTED_SCALE = 2.5

        def relu2(x):
            return jnp.square(jax.nn.relu(x))

        def _router(x2, gate_w, bias_e):
            T = x2.shape[0]
            logits = x2 @ gate_w.T
            scores = jax.nn.sigmoid(logits)
            sc = jax.lax.stop_gradient(scores + bias_e[None, :])
            grp = sc.reshape(T, N_GROUP, N_EXPERTS // N_GROUP)
            top2, _ = jax.lax.top_k(grp, 2)
            group_scores = top2.sum(-1)
            _, gidx = jax.lax.top_k(group_scores, TOPK_GROUP)
            rows = jnp.arange(T)[:, None]
            gmask = jnp.zeros((T, N_GROUP), dtype=sc.dtype).at[rows, gidx].set(1.0)
            smask = jnp.repeat(gmask, N_EXPERTS // N_GROUP, axis=1)
            masked = jnp.where(smask > 0, sc, 0.0)
            _, topk_idx = jax.lax.top_k(masked, TOP_K)
            topk_w = jnp.take_along_axis(scores, topk_idx, axis=1)
            topk_w = topk_w / (topk_w.sum(-1, keepdims=True) + 1e-20)
            topk_w = topk_w * ROUTED_SCALE
            return (topk_idx, topk_w)
        B, S, D = hidden_states.shape
        x2 = hidden_states.reshape(-1, D)
        T = x2.shape[0]
        topk_idx, topk_w = _router(x2, gate_w, bias_e)
        rows = jnp.arange(T)[:, None]
        combine = jnp.zeros((T, N_EXPERTS), dtype=topk_w.dtype).at[rows, topk_idx].add(topk_w)

        def body(acc, inp):
            wu, wd, cw = inp
            y = relu2(x2 @ wu.T) @ wd.T
            return (acc + cw[:, None] * y, None)
        routed, _ = jax.lax.scan(body, jnp.zeros_like(x2), (up_w, down_w, combine.T))
        shared = relu2(x2 @ shared_up.T) @ shared_down.T
        out = routed + shared
        return out.reshape(B, S, D)
    x = x + _L0_xattn_ref(_layernorm(x, axis=-1), ctx_768, L0_xattn_Wq, L0_xattn_bq, L0_xattn_Wk, L0_xattn_bk, L0_xattn_Wv, L0_xattn_bv)
    x = x + _L0_attn_ref(_layernorm(x, axis=-1), L0_attn_W_dq, L0_attn_W_uq, L0_attn_q_ln_g, L0_attn_q_ln_b, L0_attn_W_dkv, L0_attn_W_ukv, L0_attn_kv_ln_g, L0_attn_kv_ln_b, L0_attn_W_o)
    x = x + _L0_ffn_ref(_layernorm(x, axis=-1), L0_ffn_gate_w, L0_ffn_bias_e, L0_ffn_up_w, L0_ffn_down_w, L0_ffn_shared_up, L0_ffn_shared_down)
    return x

_drawn_inputs = setup_inputs


def setup_inputs(seed=0):
    import zlib

    import numpy as np

    out = dict(_drawn_inputs(seed))
    spreads = {'L0_attn_q_ln_g': (1.0, 0.6),
     'L0_attn_q_ln_b': (0.0, 0.8),
     'L0_attn_kv_ln_g': (1.0, 0.6),
     'L0_attn_kv_ln_b': (0.0, 0.8),
     'L0_ffn_bias_e': (0.0, 0.1)}
    factors = {'L0_xattn_bq': 37.159,
     'L0_xattn_bk': 64.0,
     'L0_attn_W_dq': 8.0,
     'L0_attn_W_uq': 8.0,
     'L0_attn_W_dkv': 4.214,
     'L0_attn_W_ukv': 4.024,
     'L0_attn_W_o': 4.633}
    for name, (base, spread) in spreads.items():
        noise = np.random.default_rng([zlib.crc32(name.encode()), seed]).standard_normal(out[name].shape)
        drawn = base * np.exp(spread * noise) if base else spread * noise
        out[name] = jnp.asarray(drawn.astype(out[name].dtype))
    for name, factor in factors.items():
        out[name] = (out[name] * factor).astype(out[name].dtype)
    return out
```

```python
from contextlib import ExitStack

import numpy as np

import concourse.bass as bass
from concourse import mybir

P = 128
F32 = mybir.dt.float32
F32R = mybir.dt.float32r
U8 = mybir.dt.uint8
ALU = mybir.AluOpType
ACT = mybir.ActivationFunctionType
AX = mybir.AxisListType
SHARED_BLOCKS = 4


def layer_program(nc, x, ctx_in, wq, wkT, wv, wd, wu, woT, experts, bq, bk, bv, gate, bias_e,
                  gammas_betas, out):
    NB, S, D = x.shape
    NKEY, TD = ctx_in.shape[1:]
    DC = D // P
    TC = TD // P
    CHUNK = 512
    KT = CHUNK // P
    NCH = NKEY // CHUNK
    G = NB * NCH
    HEADS = 16
    DH = D // HEADS
    ROWS = P // DH
    HT = HEADS // ROWS
    NX = experts.shape[0]
    NE = gate.shape[2]
    NSH = NX - NE
    IC = 2
    HALF = DC * IC * P
    T = NB * S
    GROUPS, PER, TOP_GROUPS, TOP_K, ROUTED_SCALE = 4, 4, 2, 4, 2.5
    EPS = 1e-5
    XSCALE = float(D) ** -0.5
    HSCALE = float(DH) ** -0.5
    RING = 7
    NW = 5
    W_Q, W_K, W_V, W_D, W_O = range(NW)
    assert S == P and HALF == IC * D and NE == GROUPS * PER and wd.shape[2] == 2 * P
    assert NB == 4 and HT == 4 and ROWS == 4 and NCH == KT == 4 and NSH == SHARED_BLOCKS

    with ExitStack() as es:
        def sb(name, shape, dt=F32):
            return es.enter_context(nc.sbuf_tensor(name, shape, dt))

        def at(name, shape, offset, dt=F32):
            return nc.alloc_sbuf_tensor_at(name, shape, dt, offset=offset)

        def f32(ap):
            return ap.bitcast(F32)

        def sem(name):
            return es.enter_context(nc.semaphore(name))

        ident = sb("ident", [P, P])
        upper = sb("upper", [P, P])
        lowest = sb("lowest", [P, 1])
        mhalf = sb("mhalf", [P, 2])
        earlier = sb("earlier", [P, NE, NE])
        bq_s = sb("bq_s", [P, DC])
        bk_s = sb("bk_s", [P, DC])
        bk2 = sb("bk2", [P, DC, 2], F32R)
        bv_s = sb("bv_s", [P, D])
        gate_s = sb("gate_s", [P, DC, NE])
        gate_h = sb("gate_h", [P, DC, NE], F32R)
        gate_l = sb("gate_l", [P, DC, NE], F32R)
        bias_s = sb("bias_s", [P, NE])
        gb_s = sb("gb_s", [P, 2, 2])
        res = sb("res", [P, NB, D])
        xn = sb("xn", [P, 2, D])
        xT_h = sb("xT_h", [P, DC, T], F32R)
        xT_l = sb("xT_l", [P, DC, T], F32R)
        raw = sb("raw", [P, 2, 2 * HALF])
        uw_at = -(-nc.sbuf_base // 32) * 32
        sb("uw_space", [P, 4 * HALF])
        UW = at("UW", [P, 4 * HALF], uw_at, F32R)
        DW = sb("DW", [P, 4 * HALF], F32R)
        wv_w = sb("wv_w", [P, 2, TC * D], F32R)
        qk_s = sb("qk_s", [P, 2, D])
        v_s = sb("v_s", [P, 2, D])
        hw = sb("hw", [P, 2, HEADS // ROWS * P])
        stats = sb("stats", [P, 3 * NB, 6])
        mv = sb("mv", [P, 3 * NB, 2])
        var = sb("var", [P, 3 * NB])
        rstd = sb("rstd", [P, 3 * NB])
        stats2 = sb("stats2", [P, NB, 2, 6])
        mv2 = sb("mv2", [P, NB, 2, 2])
        var2 = sb("var2", [P, NB, 2])
        rstd2 = sb("rstd2", [P, NB, 2])
        ccol = sb("ccol", [P, NB])
        xmax = sb("xmax", [P, G])
        xm = sb("xm", [P, NB])
        xnb = sb("xnb", [P, NB])
        xden = sb("xden", [P, G])
        xsum = sb("xsum", [P, NB])
        xrd = sb("xrd", [P, NB])
        hnb = sb("hnb", [P, NB, HEADS])
        hden = sb("hden", [P, NB, HEADS])
        hrd = sb("hrd", [P, NB, HEADS])

        wq_h, wq_l = UW[:, 0:2 * HALF], UW[:, 2 * HALF:4 * HALF]
        wk_h, wk_l = DW[:, 0:DC * TD], DW[:, DC * TD:2 * DC * TD]
        wu_s = at("wu_s", [P, 3 * D], uw_at)
        cf = at("cf", [P, 2, P], uw_at + 4 * 3 * D)
        hwT_first = at("hwT_first", [P, 2, HT * P], uw_at + 4 * 2 * HALF)
        onorm = at("onorm", [P, TD], uw_at + 4 * 3 * HALF)
        cqn = at("cqn", [P, 2 * P], uw_at + 4 * (3 * HALF + TD))
        oT_h, oT_l = DW[:, 2 * HALF:2 * HALF + TD], DW[:, 2 * HALF + TD:2 * HALF + 2 * TD]
        aT_first = DW[:, 2 * HALF + 2 * TD:3 * HALF + 2 * TD].rearrange("p (i t) -> p i t", i=2)
        masked = sb("masked", [P, HT * P], U8)
        wd_h, wd_l = DW[:, 0:HALF], DW[:, HALF:2 * HALF]
        u_w = [[UW[:, (2 * p + i) * HALF:(2 * p + i + 1) * HALF] for i in range(2)] for p in range(2)]
        d_w = [[DW[:, (2 * p + i) * HALF:(2 * p + i + 1) * HALF] for i in range(2)] for p in range(2)]

        start = -(-nc.sbuf_base // 32) * 32
        RING_B, CT_B, QK_B, S_B, WT_B = RING * KT * TD * 4, 4 * TC * CHUNK * 4, 2 * TC * T * 4, 2 * NKEY * 4, 2 * CHUNK * 4
        sb("arena", [P, (RING_B + CT_B + QK_B + S_B + WT_B) // 4])
        ring_at = start
        ct_at = ring_at + RING_B
        qk_at = ct_at + CT_B
        s_at = qk_at + QK_B
        wt_at = s_at + S_B

        ring = at("ring", [P, RING, KT, TD], ring_at)
        cT = at("cT", [P, 2, 2, TC, CHUNK], ct_at, F32R)
        qk_h = at("qk_h", [P, TC, T], qk_at, F32R)
        qk_l = at("qk_l", [P, TC, T], qk_at + TC * T * 4, F32R)
        sc = at("sc", [P, 2, NKEY], s_at)
        wT = at("wT", [P, 2, CHUNK], wt_at)
        qT_h = at("qT_h", [P, DC, T], s_at, F32R)
        qT_l = at("qT_l", [P, DC, T], s_at + DC * T * 4, F32R)
        wo_w = at("wo_w", [P, 2, DC * D], ct_at, F32R)
        hwT_last = at("hwT_last", [P, 2, HT * P], ring_at)
        aT_last = at("aT_last", [P, 2, HT * P], ring_at + 4096, F32R)

        def hwT(u):
            return (hwT_first if u < NB * ROWS // 2 else hwT_last)[:, u % 2, :]

        def aT(b, i):
            return (aT_first if b < NB // 2 else aT_last)[:, i, :]

        cwb = at("cwb", [P, NE, T], ring_at)
        act = at("act", [P, 2, IC, T], ring_at + 32768)
        gh = at("gh", [P, 2, IC, T], ct_at + 2 * DC * D * 4, F32R)
        gl = at("gl", [P, 2, IC, T], s_at + NB * D * 4, F32R)
        y = at("y", [P, NB, D], s_at)
        r_exp = at("r_exp", [P, NB, NE], qk_at)
        r_one = at("r_one", [P, NB, NE], qk_at + 256)
        r_sco = at("r_sco", [P, NB, NE], qk_at + 512)
        r_sc = at("r_sc", [P, NB, NE], qk_at + 768)
        r_pair = at("r_pair", [P, NB * GROUPS, 6], qk_at + 1024)
        r_gs = at("r_gs", [P, NB, GROUPS], qk_at + 1536)
        r_g1 = at("r_g1", [P, NB, GROUPS, GROUPS], qk_at + 1664)
        r_g2 = at("r_g2", [P, NB, GROUPS, GROUPS], qk_at + 1920)
        r_gr = at("r_gr", [P, NB, GROUPS], qk_at + 2176)
        r_gm = at("r_gm", [P, NB, GROUPS], qk_at + 2304)
        r_msk = at("r_msk", [P, NB, NE], qk_at + 2432)
        r_w = at("r_w", [P, NB, NE], qk_at + 2688)
        r_sum = at("r_sum", [P, NB], qk_at + 2944)
        cw = at("cw", [P, NB, NE], qk_at + 2976)
        cwT = at("cwT", [NE, T], qk_at + 3232)
        r_c1 = at("r_c1", [P, NB, NE, NE], s_at)
        r_c2 = at("r_c2", [P, NB, NE, NE], s_at + 4096)

        cw_dram = nc.dram_tensor("cw_dram", (NE, T), F32, kind="Internal").ap()
        bank = [es.enter_context(nc.psum_tensor(f"bank{i}", [P, 512], F32)) for i in range(8)]

        x_in, small_in = [sem(f"x_in{b}") for b in range(NB)], sem("small_in")
        raw_in = [sem("raw_in0"), sem("raw_in1")]
        ctx_at = [sem(f"ctx_in{i}") for i in range(RING)]
        consts = sem("consts")
        w_hi, w_lo, w_lo_pool = sem("w_hi"), sem("w_lo"), sem("w_lo_pool")
        LO_Q, LO_V, LO_D, LO_O = 1, 2, 3, 4
        u_hi, u_lo, d_hi, d_lo = sem("u_hi"), sem("u_lo"), sem("d_hi"), sem("d_lo")
        var_ok, rstd_ok, xn_ok, xT_mm, xhi_ok, xlo_ok = (sem(n) for n in ("var_ok", "rstd_ok", "xn_ok", "xT_mm", "xhi_ok", "xlo_ok"))
        small_ok, wu_in = sem("small_ok"), sem("wu_in")
        bv_ok = sem("bv_ok")
        q_mm, qhi_ok, qlo_ok, qk_mm, qkhi_ok, qklo_ok, c_mm, c_ok = (sem(n) for n in (
            "q_mm", "qhi_ok", "qlo_ok", "qk_mm", "qkhi_ok", "qklo_ok", "c_mm", "c_ok"))
        cT_mm, cThi_ok, cTlo_ok, s_mm, s_ok, xnb_ok, w_ok, wT_mm, wT_ok, o_mm, o_ok = (sem(n) for n in (
            "cT_mm", "cThi_ok", "cTlo_ok", "s_mm", "s_ok", "xnb_ok", "w_ok", "wT_mm", "wT_ok", "o_mm", "o_ok"))
        oT_mm, oThi_ok, oTlo_ok, att_mm, down_mm, var2_ok, rstd2_ok, cqn_ok, cqT_mm, cf_ok = (sem(n) for n in (
            "oT_mm", "oThi_ok", "oTlo_ok", "att_mm", "down_mm", "var2_ok", "rstd2_ok", "cqn_ok", "cqT_mm", "cf_ok"))
        qkv_mm, qkv_ok, hs_mm, hnb_ok, exp_ok, hrd_ok, hw_ok, hwT_mm, hwT_ok, a_mm, ahi_ok, alo_ok, wo_mm, x2_ok = (sem(n) for n in (
            "qkv_mm", "qkv_ok", "hs_mm", "hnb_ok", "exp_ok", "hrd_ok", "hw_ok", "hwT_mm", "hwT_ok", "a_mm", "ahi_ok", "alo_ok", "wo_mm", "x2_ok"))
        lg_mm, rexp_ok, cw_ok, cwT_mm, cwT_ok, cw_out = (sem(n) for n in ("lg_mm", "rexp_ok", "cw_ok", "cwT_mm", "cwT_ok", "cw_out"))
        CW_PARTS = (0, 2, 4, 8, NE)
        cwb_in = [sem(f"cwb_in{i}") for i in range(len(CW_PARTS) - 1)]
        up_mm, relu_ok, sq_ok, g_ok, acc_mm, y_mm, y_ok, y_out = (sem(n) for n in (
            "up_mm", "relu_ok", "sq_ok", "g_ok", "acc_mm", "y_mm", "y_ok", "y_out"))
        dve_link, pool_link = sem("dve_link"), sem("pool_link")
        IN_SLOT = (3, 2)
        NSMALL = 7
        PAIRS = (NX - 2 - NSH) // 2

        def tok(b):
            return slice(b * S, (b + 1) * S)

        LAG = 5
        POST = NCH - 1 + LAG + 1
        U_STEP = POST + 4
        UNITS = NB * ROWS
        WO_STEP = U_STEP + ROWS - 1 + 3
        STEPS = WO_STEP + NCH * (NB - 1) + 3
        B_S, B_W, B_O, B_POST, B_A = 2, 3, 4, 5, 7
        B_ACC, B_UP = (1, B_O, B_A, B_S), ((B_POST, 0), (6, B_W))

        def rows_bank(b):
            return 1 if b < NB // 2 else B_S

        FIRST = 2
        HT_TOK = T // 2
        UP_SPLIT, DOWN_SPLIT = (25, 26), (28, 30)
        UP_STEP = ((26, 27), (28, 28))
        DOWN_STEP = ((30, 31), (31, 32))

        def half_bank(e, h):
            return B_UP[e][0] if h else B_POST

        def half(h):
            return slice(h * HT_TOK, (h + 1) * HT_TOK)

        def t_bank(g, t):
            return (0, 1, 2 if g == 0 else 6 if g < U_STEP else 0)[t]

        def hs_bank(u):
            return 0 if u % 2 and U_STEP + u > G else 6

        def batch_at(step, first):
            b, r = divmod(step - first, NCH)
            return b if r == 0 and 0 <= b < NB else None

        def unit_at(step, lag):
            u = step - U_STEP - lag
            return u if 0 <= u < UNITS else None

        order = sorted([(POST + 1 + NCH * b, "middle", b) for b in range(NB)] +
                       [(WO_STEP + 1 + NCH * b, "last", b) for b in range(NB)])
        norm_no = {(kind, b): NB + i for i, (_, kind, b) in enumerate(order)}

        block = es.enter_context(nc.Block())

        @block.sync
        def _(sp):
            for b in range(NB):
                sp.dma_start(res[:, b, :], x[b]).then_inc(x_in[b], 16)
            sp.dma_start(raw[:, 0, :], wq[:, :, :].rearrange("p c n -> p (c n)")).then_inc(raw_in[0], 16)

            def load_chunk(g):
                b, c = divmod(g, NCH)
                if g >= RING:
                    sp.wait_ge(o_mm, g - RING + 1)
                src = ctx_in[b, c * CHUNK:(c + 1) * CHUNK, :].rearrange("(p k) t -> p k t", k=KT)
                sp.dma_start(ring[:, g % RING], src).then_inc(ctx_at[g % RING], 16)

            def load_item(n, src, cols):
                sp.dma_start(raw[:, n % 2, 0:cols], src.rearrange("p c n -> p (c n)")).then_inc(raw_in[n % 2], 16)

            sp.dma_start(bq_s[:], bq).then_inc(small_in, 16)
            sp.dma_start(bk_s[:], bk).then_inc(small_in, 16)
            sp.dma_start(bv_s[:], bv.partition_broadcast(P)).then_inc(small_in, 16)
            sp.dma_start(gate_s[:], gate).then_inc(small_in, 16)
            sp.dma_start(bias_s[:], bias_e.partition_broadcast(P)).then_inc(small_in, 16)
            for i in range(2):
                sp.dma_start(gb_s[:, i, :], gammas_betas[:, i, :]).then_inc(small_in, 16)
            load_chunk(0)
            load_item(W_K, wkT, DC * TD)
            for g in range(1, RING):
                load_chunk(g)
                if g == 3:
                    sp.wait_ge(w_lo, LO_Q)
                    sp.wait_ge(w_lo_pool, 1)
                    load_item(W_V, wv, TC * D)
                if g == 5:
                    sp.wait_ge(w_lo_pool, 2)
                    load_item(W_D, wd, DC * 2 * P)
            sp.wait_ge(q_mm, DC)
            sp.dma_start(wu_s[:], wu[:, :, :].rearrange("p c n -> p (c n)")).then_inc(wu_in, 16)
            sp.wait_ge(w_lo, LO_V)
            load_item(W_O, woT, DC * D)
            for g in range(RING, G):
                load_chunk(g)

            def load_expert(e, parity):
                sp.dma_start(raw[:, parity, :], experts[bass.ds(e, 1)].rearrange("e p n -> p (e n)")).then_inc(raw_in[parity], 16)

            sp.wait_ge(w_lo, LO_O)
            load_expert(0, 0)
            load_expert(1, 1)

            def load_next(e, parity):
                sp.wait_ge(u_lo, e + 1)
                sp.wait_ge(d_lo, e + 1)
                load_expert(e + 2, parity)

            for e in range(NSH - 1):
                load_next(e, e % 2)
            sp.wait_ge(cwT_ok, 1)
            sp.dma_start(cw_dram, cwT[:, :]).then_inc(cw_out, 16)
            sp.wait_ge(cw_out, 16)
            for i in range(len(CW_PARTS) - 1):
                part = slice(CW_PARTS[i], CW_PARTS[i + 1])
                sp.dma_start(cwb[:, part, :], cw_dram[part, :].partition_broadcast(P)).then_inc(cwb_in[i], 16)
                if i == 1:
                    load_next(NSH - 1, 1)
            with sp.Fori(0, PAIRS) as i:
                for p in range(2):
                    load_next(i * 2 + NSH + p, p)
            for b in range(NB):
                sp.wait_ge(y_ok, b + 1)
                sp.dma_start(out[b], y[:, b, :]).then_inc(y_out, 16)
            sp.wait_ge(y_out, 16 * NB)

        @block.gpsimd
        def _(pool):
            nc.gpsimd.memset(ident[:], 0.0).then_inc(pool_link, 1)
            nc.gpsimd.memset(upper[:], 0.0).then_inc(pool_link, 1)
            nc.gpsimd.memset(earlier[:], 1.0).then_inc(pool_link, 1)
            nc.gpsimd.memset(lowest[:], -3.4e38).then_inc(consts, 1)
            nc.gpsimd.memset(mhalf[:], -0.5).then_inc(consts, 1)
            pool.wait_ge(pool_link, 3)
            nc.gpsimd.affine_select(out=ident[:], in_=ident[:], compare_op=ALU.not_equal, fill=1.0, base=0,
                                    pattern=[[-1, P]], channel_multiplier=1).then_inc(consts, 1)
            nc.gpsimd.affine_select(out=upper[:], in_=upper[:], compare_op=ALU.is_ge, fill=1.0, base=0,
                                    pattern=[[-1, P]], channel_multiplier=1).then_inc(consts, 1)
            nc.gpsimd.affine_select(out=earlier[:], in_=earlier[:], compare_op=ALU.is_gt, fill=0.0, base=0,
                                    pattern=[[1, NE], [-1, NE]], channel_multiplier=0).then_inc(consts, 1)
            pool.wait_ge(consts, 5)

            def inverse_root(n):
                pool.wait_ge(var_ok, n + 1)
                nc.gpsimd.tensor_tensor(rstd[:, n:n + 1], var[:, n:n + 1], mhalf[:, 0:1], ALU.pow).then_inc(rstd_ok, 1)

            for n in range(NB):
                inverse_root(n)
            pool.wait_ge(w_hi, W_Q + 1)
            nc.gpsimd.tensor_tensor(wq_l[:, 0:HALF], raw[:, 0, 0:HALF], f32(wq_h[:, 0:HALF]), ALU.subtract).then_inc(w_lo_pool, 1)
            pool.wait_ge(w_hi, W_K + 1)
            nc.gpsimd.tensor_tensor(wk_l, raw[:, 1, 0:DC * TD], f32(wk_h), ALU.subtract).then_inc(w_lo_pool, 1)
            pool.wait_ge(xn_ok, NB)
            pool.wait_ge(small_in, 16 * NSMALL)
            nc.gpsimd.tensor_tensor(res[:], res[:], bv_s[:].unsqueeze(1).to_broadcast([P, NB, D]), ALU.add).then_inc(bv_ok, 1)
            for step in range(1, STEPS):
                if (b := batch_at(step, POST + 1)) is not None:
                    inverse_root(norm_no["middle", b])
                if (b := batch_at(step, POST + 2)) is not None:
                    pool.wait_ge(var2_ok, b + 1)
                    nc.gpsimd.tensor_tensor(rstd2[:, b, :], var2[:, b, :], mhalf[:, 0:2], ALU.pow).then_inc(rstd2_ok, 1)
                if (u := unit_at(step, 1)) is not None:
                    b, r = divmod(u, ROWS)
                    pool.wait_ge(hrd_ok, u + 1)
                    w3 = hw[:, u % 2, :].rearrange("p (j k) -> p j k", j=HT)
                    rd = hrd[:, b, r * HT:(r + 1) * HT].unsqueeze(2).to_broadcast([P, HT, P])
                    nc.gpsimd.tensor_tensor(w3, w3, rd, ALU.mult).then_inc(hw_ok, 1)
                if (b := batch_at(step, WO_STEP)) is not None:
                    inverse_root(norm_no["last", b])

        @block.scalar
        def _(act_e):
            copy = nc.scalar.copy

            def item_hi(n, dst, cols):
                act_e.wait_ge(raw_in[n % 2], 16 * (n // 2 + 1))
                copy(dst, raw[:, n % 2, 0:cols]).then_inc(w_hi, 1)

            def up_hi(pair, p):
                act_e.wait_ge(raw_in[p], (pair + IN_SLOT[p] + 1) * 16)
                copy(u_w[p][0], raw[:, p, 0:HALF]).then_inc(u_hi, 1)

            def down_hi(e, p):
                copy(d_w[p][0], raw[:, p, HALF:2 * HALF]).then_inc(d_hi, 1)

            def rows_hi(n, b, src):
                act_e.wait_ge(xT_mm, n + 1)
                copy(xT_h[:, :, tok(b)], src[:, :].rearrange("p (c t) -> p c t", c=DC)).then_inc(xhi_ok, 1)

            def chunk_hi(g, t):
                act_e.wait_ge(cT_mm, TC * g + t + 1)
                if g >= 2 and t == 0:
                    act_e.wait_ge(s_mm, g - 1)
                copy(cT[:, g % 2, 0, t, :], bank[t_bank(g, t)][:]).then_inc(cThi_ok, 1)

            def squares(e, p):
                for m in range(IC):
                    act_e.wait_ge(up_mm, IC * e + m + 1)
                    nc.scalar.activation(act[:, p, m, :], bank[B_UP[p][m]][:], ACT.Relu).then_inc(relu_ok, 1)
                    act_e.wait_ge(relu_ok, IC * e + m + 1)
                    nc.scalar.activation(act[:, p, m, :], act[:, p, m, :], ACT.Square).then_inc(sq_ok, 1)

            def squares_half(e, h):
                k = FIRST * h + e + 1
                a = act[:, e, :, half(h)]
                act_e.wait_ge(up_mm, k)
                nc.scalar.activation(a, bank[half_bank(e, h)][:].rearrange("p (m t) -> p m t", m=IC), ACT.Relu).then_inc(relu_ok, 1)
                act_e.wait_ge(relu_ok, k)
                nc.scalar.activation(a, a, ACT.Square).then_inc(sq_ok, 1)

            item_hi(W_Q, wq_h, 2 * HALF)
            for b in range(NB):
                rows_hi(b, b, bank[4 + b])
            item_hi(W_K, wk_h, DC * TD)
            for t in range(TC):
                chunk_hi(0, t)
            act_e.wait_ge(small_in, 16 * NSMALL)
            for j in range(DC):
                act_e.wait_ge(q_mm, j + 1)
                nc.scalar.activation(qT_h[:, j, :], bank[4 + j][:], ACT.Identity, bias=bq_s[:, j:j + 1]).then_inc(qhi_ok, 1)
            for t in range(TC):
                act_e.wait_ge(qk_mm, t + 1)
                copy(qk_h[:, t, :], bank[4 + t][:]).then_inc(qkhi_ok, 1)
            def chunk_weights(b, c):
                act_e.wait_ge(xnb_ok, b + 1)
                w = sc[:, b % 2, c * CHUNK:(c + 1) * CHUNK]
                nc.scalar.activation(w, w, ACT.Exp, bias=xnb[:, b:b + 1], scale=XSCALE,
                                     accum_out=xden[:, NCH * b + c:NCH * b + c + 1]).then_inc(w_ok, 1)

            for step in range(1, STEPS):
                if (b := batch_at(step, WO_STEP)) is not None:
                    act_e.wait_ge(a_mm, ROWS * (b + 1))
                    copy(aT(b, 0), bank[B_A][:]).then_inc(ahi_ok, 1)
                if step < G:
                    chunk_hi(step, 0)
                    chunk_hi(step, 1)
                    if step < U_STEP:
                        chunk_hi(step, 2)
                g = step - LAG
                if 0 <= g < G:
                    act_e.wait_ge(wT_mm, g + 1)
                    if g >= 2:
                        act_e.wait_ge(o_mm, g - 1)
                    copy(wT[:, g % 2, :], bank[B_W][:]).then_inc(wT_ok, 1)
                if (b := batch_at(step, POST)) is not None:
                    act_e.wait_ge(oT_mm, b + 1)
                    copy(oT_h, bank[B_POST][:, 0:TD]).then_inc(oThi_ok, 1)
                if U_STEP <= step < G:
                    chunk_hi(step, 2)
                for c in range(1, NCH):
                    if (b := batch_at(step, NCH + c)) is not None:
                        chunk_weights(b, c)
                if step == 1:
                    item_hi(W_V, wv_w[:, 0, :], TC * D)
                if step == 2:
                    item_hi(W_D, wd_h, HALF)
                if (u := unit_at(step, 2)) is not None:
                    act_e.wait_ge(hwT_mm, u + 1)
                    if u >= 2:
                        act_e.wait_ge(a_mm, u - 1)
                    copy(hwT(u), bank[B_W][:]).then_inc(hwT_ok, 1)
                if (b := batch_at(step, POST + 3)) is not None:
                    for i in (1, 0):
                        act_e.wait_ge(qkv_mm, 3 * b + 2 - i)
                        nc.scalar.activation(qk_s[:, i, :], bank[(B_S, B_POST)[i]][:], ACT.Identity,
                                             scale=(HSCALE, 1.0)[i]).then_inc(qkv_ok, 1)
                if (b := batch_at(step, WO_STEP + 1)) is not None:
                    rows_hi(norm_no["last", b], b, bank[rows_bank(b)])
                if step == G + 1:
                    act_e.wait_ge(s_mm, G)
                    item_hi(W_O, wo_w[:, 0, :], DC * D)
                for e in range(FIRST):
                    if step == UP_STEP[e][1] + 1:
                        squares_half(e, 0)
                    if step == UP_SPLIT[e]:
                        up_hi(0, e)
                    if step == DOWN_SPLIT[e]:
                        down_hi(e, e)
                if (u := unit_at(step, 0)) is not None:
                    b, r = divmod(u, ROWS)
                    act_e.wait_ge(hnb_ok, u + 1)
                    if u >= 2:
                        act_e.wait_ge(hwT_mm, u - 1)
                    for j in range(HT):
                        i = r * HT + j
                        e = nc.scalar.activation(hw[:, u % 2, j * P:(j + 1) * P], bank[hs_bank(u)][:, j * P:(j + 1) * P],
                                                 ACT.Exp, bias=hnb[:, b, i:i + 1],
                                                 accum_out=hden[:, b, i:i + 1])
                    e.then_inc(exp_ok, 1)
                if (b := batch_at(step, POST + 1)) is not None:
                    rows_hi(norm_no["middle", b], b, bank[B_POST])
                if (b := batch_at(step, POST + 2)) is not None:
                    act_e.wait_ge(cqT_mm, b + 1)
                    act_e.wait_ge(qkv_mm, 3 * b)
                    for i in range(2):
                        last = nc.scalar.activation(cf[:, i, :], bank[B_POST][:, i * P:(i + 1) * P], ACT.Identity,
                                                    bias=gb_s[:, i, 1:2], scale=gb_s[:, i, 0:1])
                    last.then_inc(cf_ok, 1)
                if (b := batch_at(step, POST + 3)) is not None:
                    act_e.wait_ge(qkv_mm, 3 * b + 3)
                    copy(v_s[:, b % 2, :], bank[B_S][:]).then_inc(qkv_ok, 1)
                if (b := batch_at(step, NCH)) is not None:
                    chunk_weights(b, 0)
                if (b := batch_at(step, WO_STEP + 2)) is not None:
                    act_e.wait_ge(lg_mm, b + 1)
                    nc.scalar.activation(r_exp[:, b, :], bank[rows_bank(b)][:, 0:NE], ACT.Exp, scale=-1.0).then_inc(rexp_ok, 1)

            for e in range(NSH):
                if e < FIRST:
                    squares_half(e, 1)
                else:
                    squares(e, e % 2)
                up_hi(e // 2 + 1, e % 2)
                if e >= 1:
                    act_e.wait_ge(acc_mm, e)
                    down_hi(e + 1, (e + 1) % 2)
            with act_e.Fori(0, PAIRS) as i:
                for p in range(2):
                    e = i * 2 + NSH + p
                    squares(e, p)
                    up_hi(i + NSH // 2 + 1, p)
                    act_e.wait_ge(acc_mm, e)
                    down_hi(e + 1, 1 - p)
            squares(NX - 2, 0)
            act_e.wait_ge(acc_mm, NX - 2)
            down_hi(NX - 1, 1)
            squares(NX - 1, 1)

        @block.vector
        def _(dve):
            V_ = nc.vector
            links = [0]

            def link(ins):
                links[0] += 1
                ins.then_inc(dve_link, 1)
                dve.wait_ge(dve_link, links[0])

            def item_lo(n, hi, lo, cols):
                dve.wait_ge(w_hi, n + 1)
                V_.tensor_tensor(lo, raw[:, n % 2, 0:cols], f32(hi), ALU.subtract).then_inc(w_lo, 1)

            def up_lo(e, p):
                dve.wait_ge(u_hi, e + 1)
                V_.tensor_tensor(u_w[p][1], raw[:, p, 0:HALF], f32(u_w[p][0]), ALU.subtract).then_inc(u_lo, 1)

            def down_lo(e, p):
                dve.wait_ge(d_hi, e + 1)
                V_.tensor_tensor(d_w[p][1], raw[:, p, HALF:2 * HALF], f32(d_w[p][0]), ALU.subtract).then_inc(d_lo, 1)

            def moments(n, b):
                link(V_.bn_stats(stats[:, n, :], res[:, b, :]))
                link(V_.bn_aggr(mv[:, n, :], stats[:, n, :]))
                V_.tensor_scalar(var[:, n:n + 1], mv[:, n, 1:2], EPS, None, ALU.add).then_inc(var_ok, 1)

            def normalise(n, b):
                if n >= 2:
                    dve.wait_ge(xT_mm, n - 1)
                dve.wait_ge(rstd_ok, n + 1)
                V_.tensor_scalar(xn[:, n % 2, :], res[:, b, :], mv[:, n, 0:1], rstd[:, n:n + 1],
                                 ALU.subtract, ALU.mult).then_inc(xn_ok, 1)

            def rows_lo(n, b, src):
                dve.wait_ge(xhi_ok, n + 1)
                V_.tensor_tensor(xT_l[:, :, tok(b)], src[:, :].rearrange("p (c t) -> p c t", c=DC),
                                 f32(xT_h[:, :, tok(b)]), ALU.subtract).then_inc(xlo_ok, 1)

            def mask_and_max(u, between=lambda: None):
                b, r = divmod(u, ROWS)
                s3 = bank[hs_bank(u)][:].rearrange("p (j k) -> p j k", j=HT)
                dve.wait_ge(hs_mm, u + 1)
                link(V_.scalar_tensor_tensor(out=masked[:].rearrange("p (j k) -> p j k", j=HT), in0=s3, scalar=0.0,
                                             in1=upper[:].unsqueeze(1).to_broadcast([P, HT, P]), op0=ALU.is_equal, op1=ALU.max))
                link(V_.copy_predicated(bank[hs_bank(u)][:], masked[:], lowest[:, 0:1].to_broadcast([P, HT * P])))
                between()
                V_.tensor_reduce(out=hnb[:, b, r * HT:(r + 1) * HT], in_=s3, op=ALU.max, axis=AX.X,
                                 negate=True).then_inc(hnb_ok, 1)

            def inverse_sums(u):
                b, r = divmod(u, ROWS)
                dve.wait_ge(exp_ok, u + 1)
                V_.reciprocal(hrd[:, b, r * HT:(r + 1) * HT], hden[:, b, r * HT:(r + 1) * HT]).then_inc(hrd_ok, 1)

            weighted, ghi_ok = sem("weighted"), sem("ghi_ok")

            def gated(e, p, routed):
                for m in range(IC):
                    k = IC * e + m + 1
                    dve.wait_ge(sq_ok, k)
                    a = act[:, p, m, :]
                    if routed:
                        V_.tensor_tensor(a, a, cwb[:, bass.ds(e - NSH, 1), :].rearrange("p e t -> p (e t)"), ALU.mult).then_inc(weighted, 1)
                        dve.wait_ge(weighted, k - IC * NSH)
                    V_.tensor_copy(gh[:, p, m, :], a).then_inc(ghi_ok, 1)
                    dve.wait_ge(ghi_ok, k)
                    V_.tensor_tensor(gl[:, p, m, :], a, f32(gh[:, p, m, :]), ALU.subtract).then_inc(g_ok, 1)

            def gated_half(e, h):
                k = FIRST * h + e + 1
                a = act[:, e, :, half(h)]
                dve.wait_ge(sq_ok, k)
                V_.tensor_copy(gh[:, e, :, half(h)], a).then_inc(ghi_ok, 1)
                dve.wait_ge(ghi_ok, k)
                V_.tensor_tensor(gl[:, e, :, half(h)], a, f32(gh[:, e, :, half(h)]), ALU.subtract).then_inc(g_ok, 1)

            def flat(t):
                return t[:].rearrange("p b e -> p (b e)")

            def ranks(dst, c1, c2, v, n):
                mine = v[:].unsqueeze(3).to_broadcast([P, NB, n, n])
                other = v[:].unsqueeze(2).to_broadcast([P, NB, n, n])
                V_.tensor_tensor(c1[:], other, mine, ALU.is_gt)
                link(V_.tensor_tensor(c2[:], other, mine, ALU.is_equal))
                link(V_.tensor_tensor(c2[:], c2[:], earlier[:, 0:n, 0:n].unsqueeze(1).to_broadcast([P, NB, n, n]), ALU.mult))
                link(V_.tensor_tensor(c1[:], c1[:], c2[:], ALU.add))
                link(V_.tensor_reduce(out=dst[:], in_=c1[:], op=ALU.add, axis=AX.X))

            def routing():
                dve.wait_ge(rexp_ok, NB)
                link(V_.tensor_scalar(flat(r_one), flat(r_exp), 1.0, None, ALU.add))
                link(V_.reciprocal(flat(r_sco), flat(r_one)))
                link(V_.tensor_tensor(r_sc[:], r_sco[:], bias_s[:].unsqueeze(1).to_broadcast([P, NB, NE]), ALU.add))
                v = r_sc[:].rearrange("p b (g e) -> p (b g) e", g=GROUPS)
                V_.tensor_tensor(r_pair[:, :, 0:3], v[:, :, 0:3], v[:, :, 1:4], ALU.add)
                V_.tensor_tensor(r_pair[:, :, 3:5], v[:, :, 0:2], v[:, :, 2:4], ALU.add)
                link(V_.tensor_tensor(r_pair[:, :, 5:6], v[:, :, 0:1], v[:, :, 3:4], ALU.add))
                link(V_.tensor_reduce(out=flat(r_gs), in_=r_pair[:], op=ALU.max, axis=AX.X))
                ranks(r_gr, r_g1, r_g2, r_gs, GROUPS)
                link(V_.tensor_scalar(flat(r_gm), flat(r_gr), float(TOP_GROUPS), None, ALU.is_lt))
                link(V_.tensor_tensor(r_msk[:].rearrange("p b (g e) -> p (b g) e", g=GROUPS), v,
                                      flat(r_gm).unsqueeze(2).to_broadcast([P, NB * GROUPS, PER]), ALU.mult))
                ranks(r_w, r_c1, r_c2, r_msk, NE)
                link(V_.scalar_tensor_tensor(out=flat(r_w), in0=flat(r_w), scalar=float(TOP_K), in1=flat(r_sco),
                                             op0=ALU.is_lt, op1=ALU.mult))
                link(V_.tensor_reduce(out=r_sum[:], in_=r_w[:], op=ALU.add, axis=AX.X))
                link(V_.tensor_scalar(r_sum[:], r_sum[:], 1e-20, None, ALU.add))
                link(V_.reciprocal(r_sum[:], r_sum[:]))
                V_.scalar_tensor_tensor(out=cw[:], in0=r_w[:], scalar=ROUTED_SCALE, in1=r_sum[:].unsqueeze(2).to_broadcast([P, NB, NE]),
                                        op0=ALU.mult, op1=ALU.mult).then_inc(cw_ok, 1)

            for b in range(NB):
                dve.wait_ge(x_in[b], 16)
                moments(b, b)
            for b in range(NB):
                normalise(b, b)
            dve.wait_ge(w_hi, W_Q + 1)
            V_.tensor_tensor(wq_l[:, HALF:2 * HALF], raw[:, 0, HALF:2 * HALF], f32(wq_h[:, HALF:2 * HALF]),
                             ALU.subtract).then_inc(w_lo, 1)
            for b in range(NB):
                rows_lo(b, b, bank[4 + b])

            def chunk_lo(g, t):
                dve.wait_ge(cThi_ok, TC * g + t + 1)
                V_.tensor_tensor(cT[:, g % 2, 1, t, :], bank[t_bank(g, t)][:], f32(cT[:, g % 2, 0, t, :]),
                                 ALU.subtract).then_inc(cTlo_ok, 1)

            dve.wait_ge(small_in, 16 * NSMALL)
            link(V_.tensor_copy(bk2[:, :, 0], bk_s[:]))
            V_.tensor_tensor(bk2[:, :, 1], bk_s[:], f32(bk2[:, :, 0]), ALU.subtract).then_inc(small_ok, 1)
            link(V_.tensor_copy(gate_h[:], gate_s[:]))
            V_.tensor_tensor(gate_l[:], gate_s[:], f32(gate_h[:]), ALU.subtract).then_inc(small_ok, 1)
            for t in range(TC):
                chunk_lo(0, t)
            for j in range(DC):
                dve.wait_ge(qhi_ok, j + 1)
                V_.scalar_tensor_tensor(out=qT_l[:, j, :], in0=bank[4 + j][:], scalar=bq_s[:, j:j + 1],
                                        in1=f32(qT_h[:, j, :]), op0=ALU.add, op1=ALU.subtract).then_inc(qlo_ok, 1)
            for t in range(TC):
                dve.wait_ge(qkhi_ok, t + 1)
                V_.tensor_tensor(qk_l[:, t, :], bank[4 + t][:], f32(qk_h[:, t, :]), ALU.subtract).then_inc(qklo_ok, 1)
            dve.wait_ge(c_mm, 1)
            V_.tensor_reduce(out=ccol[:], in_=bank[3][:, 0:2 * NB].rearrange("p (b i) -> p b i", b=NB),
                             op=ALU.add, axis=AX.X).then_inc(c_ok, 1)
            dve.wait_ge(c_ok, 1)

            for step in range(1, STEPS):
                if (b := batch_at(step, WO_STEP)) is not None:
                    dve.wait_ge(ahi_ok, b + 1)
                    V_.tensor_tensor(aT(b, 1), bank[B_A][:], f32(aT(b, 0)), ALU.subtract).then_inc(alo_ok, 1)
                if step < G:
                    chunk_lo(step, 0)
                    chunk_lo(step, 1)
                    if step < U_STEP:
                        chunk_lo(step, 2)
                if (b := batch_at(step, POST + 1)) is not None:
                    dve.wait_ge(att_mm, b + 1)
                    dve.wait_ge(bv_ok, 1)
                    link(V_.tensor_tensor(res[:, b, :], bank[B_POST][:], res[:, b, :], ALU.add))
                    moments(norm_no["middle", b], b)
                if (b := batch_at(step, WO_STEP + 1)) is not None:
                    normalise(norm_no["last", b], b)
                if (b := batch_at(step, POST)) is not None:
                    dve.wait_ge(oThi_ok, b + 1)
                    V_.tensor_tensor(oT_l, bank[B_POST][:, 0:TD], f32(oT_h), ALU.subtract).then_inc(oTlo_ok, 1)
                if (u := unit_at(step, 1)) is not None and step <= G + 1:
                    inverse_sums(u)
                b = batch_at(step, POST + 1)
                within = b is not None and G < step and unit_at(step, 0) is not None
                if (u := unit_at(step, 0)) is not None:
                    if within:
                        mask_and_max(u, lambda: normalise(norm_no["middle", b], b))
                    else:
                        mask_and_max(u)
                if (u := unit_at(step, 1)) is not None and step > G + 1 and u < UNITS - 1:
                    inverse_sums(u)
                if (b := batch_at(step, POST + 1)) is not None and not within:
                    normalise(norm_no["middle", b], b)
                g = step - 1
                if 0 <= g < G:
                    b, c = divmod(g, NCH)
                    dve.wait_ge(s_mm, g + 1)
                    if b >= 2:
                        dve.wait_ge(wT_mm, NCH * (b - 2) + c + 1)
                    V_.tensor_scalar(sc[:, b % 2, c * CHUNK:(c + 1) * CHUNK], bank[B_S][:], ccol[:, b:b + 1], None,
                                     ALU.add, ALU.max, accum_out=xmax[:, g:g + 1]).then_inc(s_ok, 1)
                    if c == NCH - 1:
                        dve.wait_ge(s_ok, g + 1)
                        link(V_.reduce_max(xm[:, b:b + 1], xmax[:, NCH * b:NCH * (b + 1)], AX.X))
                        V_.tensor_scalar(xnb[:, b:b + 1], xm[:, b:b + 1], -XSCALE, None, ALU.mult).then_inc(xnb_ok, 1)
                if U_STEP <= step < G:
                    chunk_lo(step, 2)
                if step == 1:
                    item_lo(W_V, wv_w[:, 0, :], wv_w[:, 1, :], TC * D)
                if step == 2:
                    item_lo(W_D, wd_h, wd_l, HALF)
                if (b := batch_at(step, WO_STEP + 1)) is not None:
                    rows_lo(norm_no["last", b], b, bank[rows_bank(b)])
                if (b := batch_at(step, POST + 2)) is not None:
                    dve.wait_ge(down_mm, b + 1)
                    for i in range(2):
                        last = V_.bn_stats(stats2[:, b, i, :], bank[B_POST][:, i * P:(i + 1) * P])
                    link(last)
                    for i in range(2):
                        last = V_.bn_aggr(mv2[:, b, i, :], stats2[:, b, i, :])
                    link(last)
                    V_.tensor_scalar(var2[:, b, :], mv2[:, b, :, 1], EPS, None, ALU.add).then_inc(var2_ok, 1)
                    dve.wait_ge(rstd2_ok, b + 1)
                    for i in range(2):
                        last = V_.tensor_scalar(cqn[:, i * P:(i + 1) * P], bank[B_POST][:, i * P:(i + 1) * P],
                                                mv2[:, b, i, 0:1], rstd2[:, b, i:i + 1], ALU.subtract, ALU.mult)
                    last.then_inc(cqn_ok, 1)
                if (b := batch_at(step, POST + 1)) is not None:
                    rows_lo(norm_no["middle", b], b, bank[B_POST])
                if (b := batch_at(step, POST - 1)) is not None:
                    dve.wait_ge(o_mm, NCH * (b + 1))
                    dve.wait_ge(w_ok, NCH * (b + 1))
                    link(V_.reduce_sum(xsum[:, b:b + 1], xden[:, NCH * b:NCH * (b + 1)], AX.X))
                    link(V_.reciprocal(xrd[:, b:b + 1], xsum[:, b:b + 1]))
                    if b >= 1:
                        dve.wait_ge(oT_mm, b)
                    V_.tensor_scalar(onorm[:], bank[B_O][:, 0:TD], xrd[:, b:b + 1], None, ALU.mult).then_inc(o_ok, 1)
                if (b := batch_at(step, WO_STEP)) is not None:
                    dve.wait_ge(wo_mm, b + 1)
                    V_.tensor_tensor(res[:, b, :], bank[B_S][:], res[:, b, :], ALU.add).then_inc(x2_ok, 1)
                    dve.wait_ge(x2_ok, b + 1)
                    moments(norm_no["last", b], b)
                if step == G + 1:
                    item_lo(W_O, wo_w[:, 0, :], wo_w[:, 1, :], DC * D)
                if unit_at(step, 0) == UNITS - 1:
                    inverse_sums(UNITS - 1)
                for e in range(FIRST):
                    if step == UP_STEP[e][1] + 2:
                        gated_half(e, 0)
                    if step == UP_SPLIT[e]:
                        up_lo(e, e)
                    if step == DOWN_SPLIT[e]:
                        down_lo(e, e)

            for e in range(FIRST):
                gated_half(e, 1)
                up_lo(e + 2, e)
            down_lo(FIRST, 0)
            routing()
            for e in range(FIRST, NSH):
                dve.wait_ge(acc_mm, e - 1)
                gated(e, e % 2, False)
                if e == FIRST:
                    dve.wait_ge(cwT_mm, 1)
                    V_.tensor_copy(cwT[:, :], bank[B_UP[0][0]][0:NE, :]).then_inc(cwT_ok, 1)
                up_lo(e + 2, e % 2)
                down_lo(e + 1, (e + 1) % 2)

            def routed_pair(i):
                for p in range(2):
                    e = i * 2 + NSH + p
                    dve.wait_ge(acc_mm, e - 1)
                    gated(e, p, True)
                    up_lo(e + 2, p)
                    down_lo(e + 1, 1 - p)

            dve.wait_ge(cwb_in[0], 16)
            routed_pair(0)
            for i in range(1, len(CW_PARTS) - 1):
                dve.wait_ge(cwb_in[i], 16)
            with dve.Fori(1, PAIRS) as i:
                routed_pair(i)
            dve.wait_ge(acc_mm, NX - 3)
            gated(NX - 2, 0, True)
            down_lo(NX - 1, 1)
            dve.wait_ge(acc_mm, NX - 2)
            gated(NX - 1, 1, True)
            for b in range(NB):
                dve.wait_ge(y_mm, b + 1)
                V_.tensor_tensor(y[:, b, :], bank[B_ACC[b]][:], res[:, b, :], ALU.add).then_inc(y_ok, 1)

        @block.tensor
        def _(pe):
            mm = nc.tensor.matmul

            def split_mm(dst, a, b, start, stop):
                mm(dst, a[0], b[1], start=start, stop=False)
                mm(dst, a[0], b[0], start=False, stop=False)
                return mm(dst, a[1], b[0], start=False, stop=stop)

            def rows_T(n, dst):
                pe.wait_ge(xn_ok, n + 1)
                for c in range(DC):
                    last = nc.tensor.transpose(dst[:, c * P:(c + 1) * P], xn[:, n % 2, c * P:(c + 1) * P], ident[:])
                last.then_inc(xT_mm, 1)

            pe.wait_ge(consts, 5)
            for b in range(NB):
                rows_T(b, bank[4 + b])

            def chunk_T(g, t):
                if t == 0:
                    pe.wait_ge(ctx_at[g % RING], 16 * (g // RING + 1))
                before = [TC * g_ + t_ for g_ in range(g + 1) for t_ in range(TC)
                          if TC * g_ + t_ < TC * g + t and t_bank(g_, t_) == t_bank(g, t)]
                if before:
                    pe.wait_ge(cTlo_ok, before[-1] + 1)
                elif t_bank(g, t) == 6:
                    pe.wait_ge(qklo_ok, TC)
                for k in range(KT):
                    last = nc.tensor.transpose(bank[t_bank(g, t)][:, k * P:(k + 1) * P], ring[:, g % RING, k, t * P:(t + 1) * P], ident[:])
                last.then_inc(cT_mm, 1)

            for t in range(TC):
                chunk_T(0, t)
            pe.wait_ge(w_lo, LO_Q)
            pe.wait_ge(w_lo_pool, 1)
            pe.wait_ge(xlo_ok, NB)
            for j in range(DC):
                for c in range(DC):
                    o = c * D + j * P
                    last = split_mm(bank[4 + j][:], (wq_h[:, o:o + P], wq_l[:, o:o + P]), (xT_h[:, c, :], xT_l[:, c, :]),
                                    c == 0, c == DC - 1)
                last.then_inc(q_mm, 1)
            pe.wait_ge(w_lo_pool, 2)
            for c in range(DC):
                pe.wait_ge(qlo_ok, max(c + 1, TC))
                for t in range(TC):
                    o = c * TD + t * P
                    last = split_mm(bank[4 + t][:], (wk_h[:, o:o + P], wk_l[:, o:o + P]), (qT_h[:, c, :], qT_l[:, c, :]),
                                    c == 0, c == DC - 1)
                    if c == DC - 1:
                        last.then_inc(qk_mm, 1)
            pe.wait_ge(small_ok, 2)
            for b in range(NB):
                for c in range(DC):
                    mm(bank[3][:, 2 * b:2 * b + 2], qT_h[:, c, tok(b)], bk2[:, c, :], start=c == 0, stop=False)
                    last = mm(bank[3][:, 2 * b:2 * b + 2], qT_l[:, c, tok(b)], bk2[:, c, :], start=False, stop=c == DC - 1)
            last.then_inc(c_mm, 1)

            def up(e, p, read=True):
                pe.wait_ge(u_lo, e + 1)
                for m in range(IC):
                    if read:
                        pe.wait_ge(relu_ok, IC * (e - 2) + m + 1)
                    for c in range(DC):
                        o = c * IC * P + m * P
                        last = split_mm(bank[B_UP[p][m]][:], (u_w[p][0][:, o:o + P], u_w[p][1][:, o:o + P]),
                                        (xT_h[:, c, :], xT_l[:, c, :]), c == 0, c == DC - 1)
                    last.then_inc(up_mm, 1)

            def down_tile(e, p, b, first=False, final=False):
                for m in range(IC):
                    o = m * D
                    last = split_mm(bank[B_ACC[b]][:], (gh[:, p, m, tok(b)], gl[:, p, m, tok(b)]),
                                    (d_w[p][0][:, o:o + D], d_w[p][1][:, o:o + D]), first and m == 0, final and m == IC - 1)
                return last

            def down(e, p, final=False):
                pe.wait_ge(d_lo, e + 1)
                pe.wait_ge(g_ok, IC * (e + 1))
                for b in range(NB):
                    last = down_tile(e, p, b, final=final)
                    if final:
                        last.then_inc(y_mm, 1)
                if not final:
                    last.then_inc(acc_mm, 1)

            def up_half(e, h, m):
                pe.wait_ge(u_lo, e + 1)
                for c in range(DC):
                    o = c * IC * P + m * P
                    last = split_mm(bank[half_bank(e, h)][:, m * HT_TOK:(m + 1) * HT_TOK],
                                    (u_w[e][0][:, o:o + P], u_w[e][1][:, o:o + P]),
                                    (xT_h[:, c, half(h)], xT_l[:, c, half(h)]), c == 0, c == DC - 1)
                if m == IC - 1:
                    last.then_inc(up_mm, 1)

            def first_experts(step):
                for e in range(FIRST):
                    for m in range(IC):
                        if step == UP_STEP[e][m]:
                            pe.wait_ge(xlo_ok, norm_no["last", 1] + 1)
                            if e == 0:
                                pe.wait_ge(qkv_ok, 3 * NB - 1)
                            else:
                                pe.wait_ge(relu_ok, e)
                            up_half(e, 0, m)
                    for b in range(2):
                        if step == DOWN_STEP[e][b]:
                            pe.wait_ge(d_lo, e + 1)
                            pe.wait_ge(g_ok, e + 1)
                            if e == 0:
                                pe.wait_ge(rexp_ok, 2)
                            down_tile(e, e, b, first=e == 0)

            def early(u):
                return u % ROWS != 0 and u >= ROWS + 2

            def unit_scores(u):
                b, r = divmod(u, ROWS)
                rows = slice(r * DH, (r + 1) * DH)
                pe.wait_ge(qkv_ok, 3 * b + 2)
                before = [v for v in range(u) if hs_bank(v) == hs_bank(u)]
                if before:
                    pe.wait_ge(exp_ok, before[-1] + 1)
                elif u > 0:
                    pe.wait_ge(cTlo_ok, TC * G)
                for j in range(HT):
                    o = slice(j * P, (j + 1) * P)
                    last = mm(bank[hs_bank(u)][:, o], qk_s[rows, 0, o], qk_s[rows, 1, o], start=True, stop=True)
                last.then_inc(hs_mm, 1)

            def unit_T(u, step):
                pe.wait_ge(hw_ok, u + 1)
                if step - LAG < G:
                    pe.wait_ge(wT_ok, step - LAG + 1)
                elif u >= 1:
                    pe.wait_ge(hwT_ok, u)
                for j in range(HT):
                    last = nc.tensor.transpose(bank[B_W][:, j * P:(j + 1) * P], hw[:, u % 2, j * P:(j + 1) * P], ident[:])
                last.then_inc(hwT_mm, 1)

            for step in range(1, STEPS):
                g = step
                if g < G:
                    chunk_T(g, 0)
                    chunk_T(g, 1)
                    if step < U_STEP:
                        chunk_T(g, 2)
                if (u := unit_at(step, 0)) is not None and not early(u):
                    unit_scores(u)
                g = step - LAG
                if 0 <= g < G:
                    b, c = divmod(g, NCH)
                    pe.wait_ge(w_ok, g + 1)
                    if (u := unit_at(step, 3)) is not None:
                        pe.wait_ge(hwT_ok, u + 1)
                    elif g >= 1:
                        pe.wait_ge(wT_ok, g)
                    for k in range(KT):
                        o = c * CHUNK + k * P
                        last = nc.tensor.transpose(bank[B_W][:, k * P:(k + 1) * P], sc[:, b % 2, o:o + P], ident[:])
                    last.then_inc(wT_mm, 1)
                if (b := batch_at(step, POST)) is not None:
                    pe.wait_ge(o_ok, b + 1)
                    if b >= 1:
                        pe.wait_ge(qkv_ok, 3 * b - 1)
                    for t in range(TC):
                        last = nc.tensor.transpose(bank[B_POST][:, t * P:(t + 1) * P], onorm[:, t * P:(t + 1) * P], ident[:])
                    last.then_inc(oT_mm, 1)
                g = step - 1
                if 0 <= g < G:
                    b = g // NCH
                    pe.wait_ge(cTlo_ok, TC * (g + 1))
                    if g == 0:
                        pe.wait_ge(c_ok, 1)
                        pe.wait_ge(qklo_ok, TC)
                    else:
                        pe.wait_ge(s_ok, g)
                    if (v := batch_at(step, POST + 4)) is not None:
                        pe.wait_ge(qkv_ok, 3 * v + 3)
                    for t in range(TC):
                        last = split_mm(bank[B_S][:], (qk_h[:, t, tok(b)], qk_l[:, t, tok(b)]),
                                        (cT[:, g % 2, 0, t, :], cT[:, g % 2, 1, t, :]), t == 0, t == TC - 1)
                    last.then_inc(s_mm, 1)
                if U_STEP <= step < G:
                    chunk_T(step, 2)
                if (u := unit_at(step, 2)) is not None and not G < step < G + LAG:
                    unit_T(u, step)
                if (b := batch_at(step, POST + 2)) is not None:
                    pe.wait_ge(w_lo, LO_D)
                    pe.wait_ge(xlo_ok, norm_no["middle", b] + 1)
                    for c in range(DC):
                        o = c * 2 * P
                        last = split_mm(bank[B_POST][:, 0:2 * P], (xT_h[:, c, tok(b)], xT_l[:, c, tok(b)]),
                                        (wd_h[:, o:o + 2 * P], wd_l[:, o:o + 2 * P]), c == 0, c == DC - 1)
                    last.then_inc(down_mm, 1)
                if (b := batch_at(step, POST + 3)) is not None:
                    pe.wait_ge(cf_ok, b + 1)
                    pe.wait_ge(wu_in, 16)
                    for i in (1, 0):
                        if i == 0 and step <= G:
                            pe.wait_ge(s_ok, step)
                        elif i == 0:
                            pe.wait_ge(x2_ok, b - 1)
                        for j in range(HT):
                            last = mm(bank[(B_S, B_POST)[i]][:, j * P:(j + 1) * P], wu_s[:, i * D + j * P:i * D + (j + 1) * P],
                                      cf[:, i, :], start=True, stop=True)
                        last.then_inc(qkv_mm, 1)
                if (b := batch_at(step, WO_STEP + 1)) is not None:
                    if b == 1:
                        pe.wait_ge(rexp_ok, b)
                    elif b >= 2:
                        pe.wait_ge(x2_ok, b + 1)
                    rows_T(norm_no["last", b], bank[rows_bank(b)])
                if (b := batch_at(step, WO_STEP)) is not None:
                    pe.wait_ge(w_lo, LO_O)
                    pe.wait_ge(alo_ok, b + 1)
                    if b < NB - 1:
                        pe.wait_ge(qkv_ok, 3 * (b + 2))
                    else:
                        pe.wait_ge(rexp_ok, b)
                    for j in range(HT):
                        last = split_mm(bank[B_S][:], (aT(b, 0)[:, j * P:(j + 1) * P], aT(b, 1)[:, j * P:(j + 1) * P]),
                                        (wo_w[:, 0, j * D:(j + 1) * D], wo_w[:, 1, j * D:(j + 1) * D]), j == 0, j == HT - 1)
                    last.then_inc(wo_mm, 1)
                if (u := unit_at(step, -1)) is not None and early(u):
                    unit_scores(u)
                if (u := unit_at(step, 2)) is not None and G < step < G + LAG:
                    unit_T(u, step)
                g = step - LAG
                if 0 <= g < G:
                    b, c = divmod(g, NCH)
                    pe.wait_ge(wT_ok, g + 1)
                    if c == 0 and b >= 1:
                        pe.wait_ge(o_ok, b)
                    for k in range(KT):
                        last = mm(bank[B_O][:, 0:TD], wT[:, g % 2, k * P:(k + 1) * P], ring[:, g % RING, k, :],
                                  start=(c == 0 and k == 0), stop=(c == NCH - 1 and k == KT - 1))
                    last.then_inc(o_mm, 1)
                if step <= U_STEP + UNITS + 1:
                    first_experts(step)
                if (u := unit_at(step, 2)) is not None:
                    b, r = divmod(u, ROWS)
                    rows = slice(r * DH, (r + 1) * DH)
                    pe.wait_ge(hwT_ok, u + 1)
                    pe.wait_ge(qkv_ok, 3 * b + 3)
                    if r == 0 and b >= 1:
                        pe.wait_ge(alo_ok, b)
                    for j in range(HT):
                        h = j * ROWS + r
                        last = mm(bank[B_A][rows, j * P:(j + 1) * P], v_s[:, b % 2, h * DH:(h + 1) * DH],
                                  hwT(u)[:, j * P:(j + 1) * P], start=True, stop=True)
                    last.then_inc(a_mm, 1)
                if (b := batch_at(step, POST)) is not None:
                    pe.wait_ge(w_lo, LO_V)
                    pe.wait_ge(oTlo_ok, b + 1)
                    for t in range(TC):
                        last = split_mm(bank[B_POST][:], (oT_h[:, t * P:(t + 1) * P], oT_l[:, t * P:(t + 1) * P]),
                                        (wv_w[:, 0, t * D:(t + 1) * D], wv_w[:, 1, t * D:(t + 1) * D]), t == 0, t == TC - 1)
                    last.then_inc(att_mm, 1)
                if (b := batch_at(step, POST + 1)) is not None:
                    rows_T(norm_no["middle", b], bank[B_POST])
                if (b := batch_at(step, POST + 2)) is not None:
                    pe.wait_ge(cqn_ok, b + 1)
                    for i in range(2):
                        last = nc.tensor.transpose(bank[B_POST][:, i * P:(i + 1) * P], cqn[:, i * P:(i + 1) * P], ident[:])
                    last.then_inc(cqT_mm, 1)
                if (b := batch_at(step, POST + 3)) is not None:
                    pe.wait_ge(qkv_ok, 3 * b + 2)
                    mm(bank[B_S][:], cf[:, 1, :], wu_s[:, 2 * D:3 * D], start=True, stop=True).then_inc(qkv_mm, 1)
                if (b := batch_at(step, WO_STEP + 2)) is not None:
                    pe.wait_ge(xlo_ok, norm_no["last", b] + 1)
                    for c in range(DC):
                        last = split_mm(bank[rows_bank(b)][:, 0:NE], (xT_h[:, c, tok(b)], xT_l[:, c, tok(b)]),
                                        (gate_h[:, c, :], gate_l[:, c, :]), c == 0, c == DC - 1)
                    last.then_inc(lg_mm, 1)
                if step > U_STEP + UNITS + 1:
                    first_experts(step)
            for e in range(FIRST):
                pe.wait_ge(relu_ok, FIRST)
                for m in range(IC):
                    up_half(e, 1, m)
            pe.wait_ge(rexp_ok, NB)

            def down_half(e):
                pe.wait_ge(g_ok, FIRST + e + 1)
                for b in (2, 3):
                    last = down_tile(e, e, b, first=e == 0)
                last.then_inc(acc_mm, 1)

            down_half(0)
            pe.wait_ge(relu_ok, FIRST + 1)
            up(2, 0, read=False)
            down_half(1)
            pe.wait_ge(relu_ok, FIRST + 2)
            up(3, 1, read=False)
            pe.wait_ge(cw_ok, 1)
            pe.wait_ge(relu_ok, IC * 2 + 1)
            for b in range(NB):
                last = nc.tensor.transpose(bank[B_UP[0][0]][0:NE, tok(b)], cw[:, b, :], ident[:])
            last.then_inc(cwT_mm, 1)
            down(2, 0)
            pe.wait_ge(cwT_ok, 1)
            up(4, 0)
            down(3, 1)
            with pe.Fori(0, PAIRS) as i:
                for p in range(2):
                    e = i * 2 + NSH + p
                    up(e + 1, 1 - p)
                    down(e, p)
            up(NX - 1, 1)
            down(NX - 2, 0)
            down(NX - 1, 1, final=True)


def kernel(**inputs):
    import concourse.bacc as bacc
    from concourse.bass_utils import run_bass_kernel_spmd

    a = {k: np.asarray(v) for k, v in inputs.items()}
    D = a["x"].shape[2]

    def rows(w):
        return w.reshape(-1, P, w.shape[1]).transpose(1, 0, 2)

    up_w, down_w = a["L0_ffn_up_w"], a["L0_ffn_down_w"]
    inner = up_w.shape[1]
    shared_up = a["L0_ffn_shared_up"].reshape(SHARED_BLOCKS, inner, D)
    shared_down = a["L0_ffn_shared_down"].reshape(D, SHARED_BLOCKS, inner).transpose(1, 0, 2)
    ups = np.concatenate([shared_up, up_w]).transpose(0, 2, 1)
    downs = np.concatenate([shared_down, down_w]).transpose(0, 2, 1)
    n = len(ups)
    ups = ups.reshape(n, D // P, P, inner).transpose(0, 2, 1, 3).reshape(n, P, -1)
    downs = downs.reshape(n, inner // P, P, D).transpose(0, 2, 1, 3).reshape(n, P, -1)
    gb = np.stack([a["L0_attn_q_ln_g"], a["L0_attn_q_ln_b"], a["L0_attn_kv_ln_g"], a["L0_attn_kv_ln_b"]], axis=1)
    arrays = {
        "x": a["x"],
        "ctx": a["ctx_768"],
        "wq": rows(a["L0_xattn_Wq"]),
        "wkT": rows(a["L0_xattn_Wk"].T),
        "wv": rows(a["L0_xattn_Wv"]),
        "wd": rows(np.concatenate([a["L0_attn_W_dq"], a["L0_attn_W_dkv"]], axis=1)),
        "wu": rows(np.concatenate([a["L0_attn_W_uq"], a["L0_attn_W_ukv"]], axis=1)),
        "woT": rows(a["L0_attn_W_o"].T),
        "experts": np.concatenate([ups, downs], axis=2),
        "bq": a["L0_xattn_bq"].reshape(-1, P).T,
        "bk": a["L0_xattn_bk"].reshape(-1, P).T,
        "bv": a["L0_xattn_bv"],
        "gate": rows(a["L0_ffn_gate_w"].T),
        "bias_e": a["L0_ffn_bias_e"],
        "gammas_betas": gb.reshape(P, 2, 2),
    }
    nc = bacc.Bacc("TRN2", target_bir_lowering=False, num_devices=1)
    arrays = {k: np.ascontiguousarray(v) for k, v in arrays.items()}
    aps = [nc.dram_tensor(f"in_{k}", v.shape, mybir.dt.from_np(v.dtype), kind="ExternalInput").ap() for k, v in arrays.items()]
    out = nc.dram_tensor("out_y", a["x"].shape, F32, kind="ExternalOutput").ap()
    layer_program(nc, *aps, out)
    r = run_bass_kernel_spmd(nc, [{f"in_{k}": v for k, v in arrays.items()}], core_ids=[0])
    return r.results[0]["out_y"]
```
